# Optimizing a Trainium2 kernel written in Bass

```python
import numpy as np
import jax
import jax.numpy as jnp

def _softmax(x, axis=-1):
    return jax.nn.softmax(x, axis=axis)

def _gelu(x):
    return jax.nn.gelu(x, approximate=True)

def _silu(x):
    return jax.nn.silu(x)

def _sigmoid(x):
    return jax.nn.sigmoid(x)

def _layernorm(x, axis=-1, eps=1e-05):
    m = jnp.mean(x, axis=axis, keepdims=True)
    v = jnp.var(x, axis=axis, keepdims=True)
    return (x - m) / jnp.sqrt(v + eps)

def _scatter_add(tgt, idx, src, axis=0):
    return tgt.at[idx].add(src)

def _segment_sum(src, seg, n):
    return jax.ops.segment_sum(src, seg, n)
kernel_name = 'mk_dlrm_tower_d1_rec_r8_8ea69b'

def setup_inputs(seed: int=0):
    np.random.seed(seed)
    _w = jnp.asarray

    def _rec_inputs():
        import jax
        import jax.numpy as jnp
        _tk = jax.random.key(seed)
        ids = jnp.stack([jax.random.randint(jax.random.fold_in(_tk, 200 + f), (512,), 0, v, jnp.int32) for f, v in enumerate([12500, 125000, 1000, 1250, 12500, 1250, 1250, 12500, 1250, 12500, 12500, 12500, 1000, 12500, 1000, 1250, 1000, 1250, 1250, 1000, 1250, 12500, 1000, 1000, 1000, 1000])], axis=1)
        tbl_0 = 0.05 * jax.random.normal(jax.random.fold_in(_tk, 500 + 0), (12500, 128), jnp.float32)
        tbl_1 = 0.05 * jax.random.normal(jax.random.fold_in(_tk, 500 + 1), (125000, 128), jnp.float32)
        tbl_2 = 0.05 * jax.random.normal(jax.random.fold_in(_tk, 500 + 2), (1000, 128), jnp.float32)
        tbl_3 = 0.05 * jax.random.normal(jax.random.fold_in(_tk, 500 + 3), (1250, 128), jnp.float32)
        tbl_4 = 0.05 * jax.random.normal(jax.random.fold_in(_tk, 500 + 4), (12500, 128), jnp.float32)
        tbl_5 = 0.05 * jax.random.normal(jax.random.fold_in(_tk, 500 + 5), (1250, 128), jnp.float32)
        tbl_6 = 0.05 * jax.random.normal(jax.random.fold_in(_tk, 500 + 6), (1250, 128), jnp.float32)
        tbl_7 = 0.05 * jax.random.normal(jax.random.fold_in(_tk, 500 + 7), (12500, 128), jnp.float32)
        tbl_8 = 0.05 * jax.random.normal(jax.random.fold_in(_tk, 500 + 8), (1250, 128), jnp.float32)
        tbl_9 = 0.05 * jax.random.normal(jax.random.fold_in(_tk, 500 + 9), (12500, 128), jnp.float32)
        tbl_10 = 0.05 * jax.random.normal(jax.random.fold_in(_tk, 500 + 10), (12500, 128), jnp.float32)
        tbl_11 = 0.05 * jax.random.normal(jax.random.fold_in(_tk, 500 + 11), (12500, 128), jnp.float32)
        tbl_12 = 0.05 * jax.random.normal(jax.random.fold_in(_tk, 500 + 12), (1000, 128), jnp.float32)
        tbl_13 = 0.05 * jax.random.normal(jax.random.fold_in(_tk, 500 + 13), (12500, 128), jnp.float32)
        tbl_14 = 0.05 * jax.random.normal(jax.random.fold_in(_tk, 500 + 14), (1000, 128), jnp.float32)
        tbl_15 = 0.05 * jax.random.normal(jax.random.fold_in(_tk, 500 + 15), (1250, 128), jnp.float32)
        tbl_16 = 0.05 * jax.random.normal(jax.random.fold_in(_tk, 500 + 16), (1000, 128), jnp.float32)
        tbl_17 = 0.05 * jax.random.normal(jax.random.fold_in(_tk, 500 + 17), (1250, 128), jnp.float32)
        tbl_18 = 0.05 * jax.random.normal(jax.random.fold_in(_tk, 500 + 18), (1250, 128), jnp.float32)
        tbl_19 = 0.05 * jax.random.normal(jax.random.fold_in(_tk, 500 + 19), (1000, 128), jnp.float32)
        tbl_20 = 0.05 * jax.random.normal(jax.random.fold_in(_tk, 500 + 20), (1250, 128), jnp.float32)
        tbl_21 = 0.05 * jax.random.normal(jax.random.fold_in(_tk, 500 + 21), (12500, 128), jnp.float32)
        tbl_22 = 0.05 * jax.random.normal(jax.random.fold_in(_tk, 500 + 22), (1000, 128), jnp.float32)
        tbl_23 = 0.05 * jax.random.normal(jax.random.fold_in(_tk, 500 + 23), (1000, 128), jnp.float32)
        tbl_24 = 0.05 * jax.random.normal(jax.random.fold_in(_tk, 500 + 24), (1000, 128), jnp.float32)
        tbl_25 = 0.05 * jax.random.normal(jax.random.fold_in(_tk, 500 + 25), (1000, 128), jnp.float32)
        _rk = jax.random.fold_in(_tk, 7)
        r_dense_x = -0.000514642 + 1.00011 * jax.random.normal(jax.random.fold_in(_rk, 101), (512, 128), jnp.float32)
        W_top1 = 0.0456912 * jax.random.normal(jax.random.fold_in(_tk, 801), (479, 512), jnp.float32)
        W_top2 = 0.0441942 * jax.random.normal(jax.random.fold_in(_tk, 802), (512, 256), jnp.float32)
        W_top3 = 0.0625 * jax.random.normal(jax.random.fold_in(_tk, 803), (256, 1), jnp.float32)
        b_top1 = jnp.zeros((512,), jnp.float32)
        b_top2 = jnp.zeros((256,), jnp.float32)
        return (r_dense_x, ids, tbl_0, tbl_1, tbl_2, tbl_3, tbl_4, tbl_5, tbl_6, tbl_7, tbl_8, tbl_9, tbl_10, tbl_11, tbl_12, tbl_13, tbl_14, tbl_15, tbl_16, tbl_17, tbl_18, tbl_19, tbl_20, tbl_21, tbl_22, tbl_23, tbl_24, tbl_25, W_top1, b_top1, W_top2, b_top2, W_top3)
    r_dense_x, ids, tbl_0, tbl_1, tbl_2, tbl_3, tbl_4, tbl_5, tbl_6, tbl_7, tbl_8, tbl_9, tbl_10, tbl_11, tbl_12, tbl_13, tbl_14, tbl_15, tbl_16, tbl_17, tbl_18, tbl_19, tbl_20, tbl_21, tbl_22, tbl_23, tbl_24, tbl_25, W_top1, b_top1, W_top2, b_top2, W_top3 = _rec_inputs()

    def _L0_rec_setup():
        import jax, jax.numpy as jnp
        import numpy as np
        F = 26
        D = 128
        B = 2048
        _TRIU_I, _TRIU_J = np.triu_indices(F + 1, k=1)
        _TRIU_I = jnp.asarray(_TRIU_I)
        _TRIU_J = jnp.asarray(_TRIU_J)
        key = jax.random.key(seed)
        k1, k2 = jax.random.split(key)
        sparse_x = jax.random.normal(k1, (B, F, D), dtype=jnp.float32)
        dense_x = jax.random.normal(k2, (B, D), dtype=jnp.float32)
        return {'sparse_x': sparse_x, 'dense_x': dense_x}
    _L0_rec_all = _L0_rec_setup()
    _L0_rec_in = {k: v for k, v in _L0_rec_all.items() if k in ()}
    del _L0_rec_all
    return {'r_dense_x': r_dense_x, 'ids': ids, 'tbl_0': tbl_0, 'tbl_1': tbl_1, 'tbl_2': tbl_2, 'tbl_3': tbl_3, 'tbl_4': tbl_4, 'tbl_5': tbl_5, 'tbl_6': tbl_6, 'tbl_7': tbl_7, 'tbl_8': tbl_8, 'tbl_9': tbl_9, 'tbl_10': tbl_10, 'tbl_11': tbl_11, 'tbl_12': tbl_12, 'tbl_13': tbl_13, 'tbl_14': tbl_14, 'tbl_15': tbl_15, 'tbl_16': tbl_16, 'tbl_17': tbl_17, 'tbl_18': tbl_18, 'tbl_19': tbl_19, 'tbl_20': tbl_20, 'tbl_21': tbl_21, 'tbl_22': tbl_22, 'tbl_23': tbl_23, 'tbl_24': tbl_24, 'tbl_25': tbl_25, 'W_top1': W_top1, 'b_top1': b_top1, 'W_top2': W_top2, 'b_top2': b_top2, 'W_top3': W_top3}

def reference(r_dense_x, ids, tbl_0, tbl_1, tbl_2, tbl_3, tbl_4, tbl_5, tbl_6, tbl_7, tbl_8, tbl_9, tbl_10, tbl_11, tbl_12, tbl_13, tbl_14, tbl_15, tbl_16, tbl_17, tbl_18, tbl_19, tbl_20, tbl_21, tbl_22, tbl_23, tbl_24, tbl_25, W_top1, b_top1, W_top2, b_top2, W_top3):
    import jax
    import jax.numpy as jnp

    def _L0_rec_ref(sparse_x, dense_x):
        import jax, jax.numpy as jnp
        import numpy as np
        F = 26
        D = 128
        B = 2048
        _TRIU_I, _TRIU_J = np.triu_indices(F + 1, k=1)
        _TRIU_I = jnp.asarray(_TRIU_I)
        _TRIU_J = jnp.asarray(_TRIU_J)
        combined = jnp.concatenate([sparse_x, dense_x[:, None, :]], axis=1)
        interact = jnp.einsum('bfd,bgd->bfg', combined, combined)
        return interact[:, _TRIU_I, _TRIU_J]
    e = jnp.stack([tbl_0[ids[:, 0]], tbl_1[ids[:, 1]], tbl_2[ids[:, 2]], tbl_3[ids[:, 3]], tbl_4[ids[:, 4]], tbl_5[ids[:, 5]], tbl_6[ids[:, 6]], tbl_7[ids[:, 7]], tbl_8[ids[:, 8]], tbl_9[ids[:, 9]], tbl_10[ids[:, 10]], tbl_11[ids[:, 11]], tbl_12[ids[:, 12]], tbl_13[ids[:, 13]], tbl_14[ids[:, 14]], tbl_15[ids[:, 15]], tbl_16[ids[:, 16]], tbl_17[ids[:, 17]], tbl_18[ids[:, 18]], tbl_19[ids[:, 19]], tbl_20[ids[:, 20]], tbl_21[ids[:, 21]], tbl_22[ids[:, 22]], tbl_23[ids[:, 23]], tbl_24[ids[:, 24]], tbl_25[ids[:, 25]]], axis=1)
    z = _L0_rec_ref(e, r_dense_x)
    z = z.reshape(z.shape[0], -1)
    h = jnp.concatenate([z, r_dense_x], axis=1)
    h = jnp.maximum(h @ W_top1 + b_top1, 0.0)
    h = jnp.maximum(h @ W_top2 + b_top2, 0.0)
    y = h @ W_top3
    return y

_drawn_inputs = setup_inputs


def setup_inputs(seed=0):
    import zlib

    import numpy as np

    out = dict(_drawn_inputs(seed))
    spreads = {'b_top1': (0.0, 0.1), 'b_top2': (0.0, 0.1)}
    factors = {}
    for name, (base, spread) in spreads.items():
        noise = np.random.default_rng([zlib.crc32(name.encode()), seed]).standard_normal(out[name].shape)
        drawn = base * np.exp(spread * noise) if base else spread * noise
        out[name] = jnp.asarray(drawn.astype(out[name].dtype))
    for name, factor in factors.items():
        out[name] = (out[name] * factor).astype(out[name].dtype)
    return out
```

```python
from contextlib import ExitStack

import concourse.bass as bass
from concourse import mybir

BATCH, DIM, FIELDS = 512, 128, 26
ROWS = [12500, 125000, 1000, 1250, 12500, 1250, 1250, 12500, 1250, 12500, 12500, 12500, 1000,
        12500, 1000, 1250, 1000, 1250, 1250, 1000, 1250, 12500, 1000, 1000, 1000, 1000]
H1, H2 = 512, 256

P = 128
TILE = 128
TILES = BATCH // TILE
FEATURES = FIELDS + 1
SLOT = 32
QUAD = 4

PICKED = [f for f in range(FIELDS) if ROWS[f] == 1000][:6]
PICK_ROWS = 1000
CHUNKS = 8
PICK_P = PICK_ROWS // CHUNKS
GATHERED = [f for f in range(FIELDS) if f not in PICKED]
ORDER = PICKED + [FIELDS] + GATHERED
PICKS = len(PICKED)
DENSE_AT = PICKS
FIRST_GATHERED = PICKS + 1

QUADS = [list(range(a, min(a + QUAD, FIRST_GATHERED))) for a in range(0, FIRST_GATHERED, QUAD)]
EARLY_QUADS = len(QUADS)
QUADS += [list(range(a, min(a + QUAD, FEATURES))) for a in range(FIRST_GATHERED, FEATURES, QUAD)]
NQ = len(QUADS)

GROUPS = TILE // QUAD
CHUNK_GROUPS = 8
GRAM_CHUNKS = GROUPS // CHUNK_GROUPS
COLS = FEATURES - 1
SHIFT = (-COLS) % QUAD
STEPS = (COLS + SHIFT) // QUAD
K1 = H1 // P
K2 = H2 // P


def pair_rows():
    index = {}
    for i in range(FEATURES):
        for j in range(i + 1, FEATURES):
            index[i, j] = len(index)
    rows = []
    for step in range(STEPS):
        for block in range(QUAD):
            g = step * QUAD + block - SHIFT + 1
            for f in range(SLOT):
                pair = f < g and g >= 1
                rows.append(index[tuple(sorted((ORDER[f], ORDER[g])))] if pair else -1)
    return rows


def build(nc, x, ids, ids_by_field, tables, w1, b1, w2, b2, w3, out):
    fp32, fp32r, i32, u32 = mybir.dt.float32, mybir.dt.float32r, mybir.dt.int32, mybir.dt.uint32
    ALU, ACT = mybir.AluOpType, mybir.ActivationFunctionType

    with ExitStack() as ctx:
        def sb(name, shape, dt=fp32):
            return ctx.enter_context(nc.sbuf_tensor(name, shape, dt))

        def sem(name):
            return ctx.enter_context(nc.semaphore(name))

        ids_sb = sb("ids_sb", [P, TILES, FIELDS], i32)
        ids_row = sb("ids_row", [PICK_P, PICKS, BATCH], i32)
        row_of = sb("row_of", [PICK_P, CHUNKS], i32)
        table = sb("table", [PICK_P, PICKS, CHUNKS, DIM])
        table_hi = sb("table_hi", [PICK_P, PICKS, CHUNKS, DIM], fp32r)
        table_lo = sb("table_lo", [PICK_P, PICKS, CHUNKS, DIM], fp32r)
        onehot = sb("onehot", [PICK_P, PICKS, CHUNKS, TILE], fp32r)
        rows = sb("rows", [P, FEATURES, DIM])
        ident = sb("ident", [P, P])
        xT = sb("xT", [P, GROUPS, QUAD, SLOT])
        pairs = sb("pairs", [P, STEPS, TILE])
        w1_pairs = sb("w1_pairs", [P, STEPS, H1])
        w1_dense = sb("w1_dense", [P, H1])
        w2_sb = sb("w2_sb", [P, K1, H2])
        w3_sb = sb("w3_sb", [P, K2])
        b1_sb = sb("b1_sb", [P, K1])
        b2_sb = sb("b2_sb", [P, K2])
        xdT = sb("xdT", [P, TILE])
        h1 = sb("h1", [P, K1, TILE])
        h2 = sb("h2", [P, K2, TILE])
        y_all = sb("y_all", [1, BATCH])

        tr = [ctx.enter_context(nc.psum_tensor(f"tr{i}", [P, QUAD, TILE], fp32)) for i in range(2)]
        gram = [ctx.enter_context(nc.psum_tensor(f"gram{i}", [P, CHUNK_GROUPS, P], fp32)) for i in range(2)]
        h1_ps = [ctx.enter_context(nc.psum_tensor(f"h1_ps{i}", [P, 512], fp32)) for i in range(2)]
        h2_ps = [gram[0][:, 4 * m, :] for m in range(K2)]
        y_ps = h1_ps[1][0:1, 2 * TILE:3 * TILE]

        ids_in = sem("ids_in")
        ids_row_in = sem("ids_row_in")
        table_in = [sem(f"table_in{i}") for i in range(PICKS)]
        w1_in = sem("w1_in")
        w_in = sem("w_in")
        dense_in = sem("dense_in")
        gathered = [sem(f"gathered{k}") for k in range(NQ - EARLY_QUADS)]
        ident_made = sem("ident_made")
        row_of_made = sem("row_of_made")
        pads_zeroed = sem("pads_zeroed")
        hi_made = sem("hi_made")
        lo_made = sem("lo_made")
        onehot_made = sem("onehot_made")
        quad_ready = sem("quad_ready")
        quad_taken = sem("quad_taken")
        xdT_made = sem("xdT_made")
        gram_ready = sem("gram_ready")
        gram_taken_v = sem("gram_taken_v")
        gram_taken_s = sem("gram_taken_s")
        h1_ready = sem("h1_ready")
        h1_made = sem("h1_made")
        h2_ready = sem("h2_ready")
        h2_made = sem("h2_made")
        y_ready = sem("y_ready")
        y_taken = sem("y_taken")
        out_done = sem("out_done")
        block = ctx.enter_context(nc.Block())

        @block.sync
        def _(sp):
            def load_dense(t):
                sp.dma_start(rows[:, DENSE_AT, :], x[bass.ts(t, TILE), :]).then_inc(dense_in, 16)

            sp.dma_start(ids_sb[:, :, :], ids.rearrange("(t p) f -> p t f", p=TILE)).then_inc(ids_in, 16)
            for i, f in enumerate(PICKED):
                sp.dma_start(ids_row[:, i, :],
                             ids_by_field[f:f + 1, :].to_broadcast([PICK_P, BATCH])).then_inc(ids_row_in, 16)
                sp.dma_start(table[:, i, :, :],
                             tables[f].rearrange("(p c) d -> p c d", c=CHUNKS)).then_inc(table_in[i], 16)
                if i == 0:
                    load_dense(0)
            with sp.Fori(1, TILES) as t:
                sp.wait_ge(quad_ready, t * NQ - NQ + EARLY_QUADS)
                load_dense(t)
            sp.wait_ge(y_taken, TILES)
            sp.dma_start(out.rearrange("b o -> o b"), y_all[:, :]).then_inc(out_done, 16)
            sp.wait_ge(out_done, 16)

        @block.gpsimd
        def _(pool):
            nc.gpsimd.iota(row_of[:, :], [[1, CHUNKS]], base=0, channel_multiplier=CHUNKS).then_inc(row_of_made, 1)
            nc.gpsimd.memset(ident[:, :], 1.0).then_inc(ident_made, 1)
            pool.wait_ge(ident_made, 1)
            nc.gpsimd.affine_select(out=ident[:, :], in_=ident[:, :], compare_op=ALU.is_equal, fill=0.0,
                                    base=0, pattern=[[-1, P]], channel_multiplier=1).then_inc(ident_made, 1)

            pool.wait_ge(ids_in, 16)
            for t in range(TILES):
                for k, at in enumerate(QUADS[EARLY_QUADS:]):
                    if t >= 1:
                        pool.wait_ge(quad_ready, (t - 1) * NQ + EARLY_QUADS + k + 1)
                    for i in at:
                        nc.gpsimd.indirect_dma_start(
                            rows[:, i, :], None, tables[ORDER[i]],
                            bass.IndirectOffsetOnAxis(ap=ids_sb[:, t, ORDER[i]:ORDER[i] + 1].bitcast(u32), axis=0),
                        ).then_inc(gathered[k], 16)

        def move_blocks(copy, chunk, samples):
            for s in samples:
                for block_ in range(QUAD):
                    first = 1 if block_ < SHIFT else 0
                    col = s * COLS + first * QUAD + block_ - SHIFT
                    src = gram[chunk % 2][SLOT * s:SLOT * (s + 1), :, col:s * COLS + COLS:QUAD]
                    at = s * GROUPS + chunk * CHUNK_GROUPS
                    dst = pairs[SLOT * block_:SLOT * (block_ + 1), first:STEPS, at:at + CHUNK_GROUPS]
                    last = copy(dst, src.rearrange("p t q -> p q t"))
            return last

        @block.scalar
        def _(act):
            act.dma_start(w1_pairs[:, :, :], w1[0:STEPS * P, :].rearrange("(q p) n -> p q n", p=P)).then_inc(w1_in, 16)
            act.dma_start(w1_dense[:, :], w1[STEPS * P:, :]).then_inc(w1_in, 16)
            act.dma_start(w2_sb[:, :, :], w2.rearrange("(q p) n -> p q n", p=P)).then_inc(w_in, 16)
            act.dma_start(w3_sb[:, :], w3).then_inc(w_in, 16)
            act.dma_start(b1_sb[:, :], b1).then_inc(w_in, 16)
            act.dma_start(b2_sb[:, :], b2).then_inc(w_in, 16)
            for i in range(PICKS):
                act.wait_ge(table_in[i], 16)
                nc.scalar.copy(table_hi[:, i, :, :], table[:, i, :, :]).then_inc(hi_made, 1)

            with act.Fori(0, TILES) as t:
                for q, at in enumerate(QUADS):
                    act.wait_ge(quad_ready, t * NQ + q + 1)
                    bank = tr[q % 2]
                    if DENSE_AT in at:
                        nc.scalar.copy(xdT[:, :], bank[:, DENSE_AT - at[0], :])
                    nc.scalar.copy(
                        xT[:, :, :, at[0]:at[0] + len(at)].rearrange("p g s f -> p s g f"),
                        bank[:, 0:len(at), :].rearrange("p f (s g) -> p s g f", s=QUAD)).then_inc(quad_taken, 1)
                for chunk in range(GRAM_CHUNKS):
                    act.wait_ge(gram_ready, t * GRAM_CHUNKS + chunk + 1)
                    move_blocks(nc.scalar.copy, chunk, (2, 3)).then_inc(gram_taken_s, 1)

        @block.vector
        def _(dve):
            nc.vector.memset(xT[:, :, :, FEATURES:SLOT], 0.0).then_inc(pads_zeroed, 1)

            def make_onehot(t, i):
                nc.vector.tensor_tensor(
                    onehot[:, i, :, :],
                    ids_row[:, i, bass.ts(t, TILE)].unsqueeze(1).to_broadcast([PICK_P, CHUNKS, TILE]),
                    row_of[:, :].unsqueeze(2).to_broadcast([PICK_P, CHUNKS, TILE]),
                    ALU.is_equal).then_inc(onehot_made, 1)

            dve.wait_ge(ids_row_in, 16 * PICKS)
            dve.wait_ge(row_of_made, 1)
            for i in range(PICKS):
                make_onehot(0, i)
                dve.wait_ge(hi_made, i + 1)
                nc.vector.tensor_tensor(table_lo[:, i, :, :], table[:, i, :, :],
                                        table_hi[:, i, :, :].bitcast(fp32), ALU.subtract).then_inc(lo_made, 1)
            dve.wait_ge(w_in, 16 * 4)

            def tile(t, more):
                for chunk in range(GRAM_CHUNKS):
                    dve.wait_ge(gram_ready, t * GRAM_CHUNKS + chunk + 1)
                    move_blocks(nc.vector.tensor_copy, chunk, (0, 1)).then_inc(gram_taken_v, 1)
                for half in range(2):
                    for i in range(half * PICKS // 2, (half + 1) * PICKS // 2) if more else ():
                        make_onehot(t + 1, i)
                    dve.wait_ge(h1_ready, 2 * t + half + 1)
                    for n in (0, 1):
                        k = 2 * half + n
                        last = nc.vector.tensor_scalar(h1[:, k, :], h1_ps[half][:, n * TILE:(n + 1) * TILE],
                                                       b1_sb[:, k:k + 1], 0.0, ALU.add, ALU.max)
                    last.then_inc(h1_made, 1)
                for m in range(K2):
                    dve.wait_ge(h2_ready, K2 * t + m + 1)
                    nc.vector.tensor_scalar(h2[:, m, :], h2_ps[m], b2_sb[:, m:m + 1], 0.0,
                                            ALU.add, ALU.max).then_inc(h2_made, 1)
                dve.wait_ge(y_ready, t + 1)
                nc.vector.tensor_copy(y_all[:, bass.ts(t, TILE)], y_ps).then_inc(y_taken, 1)

            with dve.Fori(0, TILES - 1) as t:
                tile(t, True)
            tile(TILES - 1, False)

        @block.tensor
        def _(pe):
            pe.wait_ge(ident_made, 2)
            pe.wait_ge(pads_zeroed, 1)

            with pe.Fori(0, TILES) as t:
                for q, at in enumerate(QUADS):
                    bank = tr[q % 2]
                    if q >= 2:
                        pe.wait_ge(quad_taken, t * NQ + q - 1)
                    if q >= EARLY_QUADS:
                        pe.wait_ge(gathered[q - EARLY_QUADS], t * (16 * len(at)) + 16 * len(at))
                    for n, i in enumerate(at):
                        if i < PICKS:
                            pe.wait_ge(lo_made, i + 1)
                            pe.wait_ge(onehot_made, t * PICKS + i + 1)
                            for c in range(CHUNKS):
                                for part, tab in enumerate((table_hi, table_lo)):
                                    last = nc.tensor.matmul(bank[:, n, :], tab[:, i, c, :], onehot[:, i, c, :],
                                                            start=(c == 0 and part == 0),
                                                            stop=(c == CHUNKS - 1 and part == 1))
                        else:
                            if i == DENSE_AT:
                                pe.wait_ge(dense_in, t * 16 + 16)
                            last = nc.tensor.transpose(bank[:, n, :], rows[:, i, :], ident[:, :])
                    last.then_inc(quad_ready, 1)
                pe.wait_ge(quad_taken, t * NQ + NQ)
                for chunk in range(GRAM_CHUNKS):
                    if chunk >= 2:
                        pe.wait_ge(gram_taken_v, t * GRAM_CHUNKS + chunk - 1)
                        pe.wait_ge(gram_taken_s, t * GRAM_CHUNKS + chunk - 1)
                    for n in range(CHUNK_GROUPS):
                        g = chunk * CHUNK_GROUPS + n
                        last = nc.tensor.matmul(gram[chunk % 2][:, n, 0:QUAD * COLS], xT[:, g, :, :],
                                                xT[:, g, :, 1:FEATURES], start=True, stop=True)
                    last.then_inc(gram_ready, 1)
                pe.wait_ge(gram_taken_v, t * GRAM_CHUNKS + GRAM_CHUNKS)
                pe.wait_ge(gram_taken_s, t * GRAM_CHUNKS + GRAM_CHUNKS)
                pe.wait_ge(w1_in, 16 * 2)
                for k in range(K1):
                    dst = h1_ps[k // 2][:, (k % 2) * TILE:(k % 2 + 1) * TILE]
                    for q in range(STEPS):
                        low = SLOT * SHIFT if q == 0 else 0
                        nc.tensor.matmul(dst, w1_pairs[low:P, q, k * P:(k + 1) * P], pairs[low:P, q, :],
                                         start=(q == 0), stop=False)
                    last = nc.tensor.matmul(dst, w1_dense[:, k * P:(k + 1) * P], xdT[:, :], start=False, stop=True)
                    if k % 2:
                        last.then_inc(h1_ready, 1)
                pe.wait_ge(w_in, 16 * 4)
                for k in range(K1):
                    if k % 2 == 0:
                        pe.wait_ge(h1_made, t * 2 + k // 2 + 1)
                    for m in range(K2):
                        last = nc.tensor.matmul(h2_ps[m], w2_sb[:, k, m * P:(m + 1) * P], h1[:, k, :],
                                                start=(k == 0), stop=(k == K1 - 1))
                        if k == K1 - 1:
                            last.then_inc(h2_ready, 1)
                for m in range(K2):
                    pe.wait_ge(h2_made, t * K2 + m + 1)
                    last = nc.tensor.matmul(y_ps, w3_sb[:, m:m + 1], h2[:, m, :], start=(m == 0), stop=(m == K2 - 1))
                last.then_inc(y_ready, 1)


def kernel(**inputs):
    import numpy as np
    import concourse.bacc as bacc
    from concourse.bass_utils import run_bass_kernel_spmd

    nc = bacc.Bacc("TRN2", target_bir_lowering=False, num_devices=1)
    arrays = {}

    def dram(name, a):
        a = np.ascontiguousarray(a)
        arrays[f"in_{name}_dram"] = a
        return nc.dram_tensor(f"in_{name}_dram", a.shape, mybir.dt.from_np(a.dtype), kind="ExternalInput").ap()

    ids = np.asarray(inputs["ids"])
    w1 = np.asarray(inputs["W_top1"])
    chosen = np.array(pair_rows())
    n_pairs = FEATURES * (FEATURES - 1) // 2
    w1_padded = np.zeros((STEPS * P + DIM, H1), w1.dtype)
    w1_padded[np.flatnonzero(chosen >= 0)] = w1[chosen[chosen >= 0]]
    w1_padded[STEPS * P:] = w1[n_pairs:]

    def by_partition(v):
        return np.asarray(v).reshape(-1, P).T

    out = nc.dram_tensor("out_dram", (BATCH, 1), mybir.dt.float32, kind="ExternalOutput").ap()
    build(nc, dram("x", inputs["r_dense_x"]), dram("ids", ids), dram("ids_by_field", ids.T),
          [dram(f"tbl_{f}", inputs[f"tbl_{f}"]) for f in range(FIELDS)],
          dram("w1", w1_padded), dram("b1", by_partition(inputs["b_top1"])), dram("w2", inputs["W_top2"]),
          dram("b2", by_partition(inputs["b_top2"])), dram("w3", by_partition(inputs["W_top3"])), out)
    r = run_bass_kernel_spmd(nc, [arrays], core_ids=[0])
    return r.results[0]["out_dram"]
```

```python
from contextlib import ExitStack

import concourse.bass as bass
from concourse import mybir

BATCH, DIM, FIELDS = 512, 128, 26
ROWS = [12500, 125000, 1000, 1250, 12500, 1250, 1250, 12500, 1250, 12500, 12500, 12500, 1000,
        12500, 1000, 1250, 1000, 1250, 1250, 1000, 1250, 12500, 1000, 1000, 1000, 1000]
H1, H2 = 512, 256

P = 128
TILE = 128
TILES = BATCH // TILE
FEATURES = FIELDS + 1
SLOT = 32
QUAD = 4

PICKED = [f for f in range(FIELDS) if ROWS[f] == 1000][:6]
PICK_ROWS = 1000
CHUNKS = 8
PICK_P = PICK_ROWS // CHUNKS
GATHERED = [f for f in range(FIELDS) if f not in PICKED]
ORDER = PICKED + [FIELDS] + GATHERED
PICKS = len(PICKED)
RING = 3
DENSE_AT = PICKS

QUADS = [list(range(a, min(a + QUAD, FEATURES - 1))) for a in range(DENSE_AT, FEATURES - 1, QUAD)]
QUADS += [[FEATURES - 1]]
NQ = len(QUADS)

GROUPS = TILE // QUAD
CHUNK_GROUPS = 8
GRAM_CHUNKS = GROUPS // CHUNK_GROUPS
HALF = (FEATURES - 1) // 2
MERGED = HALF + 1
SHIFT = (-MERGED) % QUAD
STEPS = (MERGED + SHIFT) // QUAD
K1 = H1 // P
K2 = H2 // P


def from_second(m, f):
    return m >= 1 and m <= f < m + HALF


def pair_rows():
    index = {}
    for i in range(FEATURES):
        for j in range(i + 1, FEATURES):
            index[i, j] = len(index)
    rows = []
    for at in range(STEPS * QUAD):
        m = at - SHIFT
        for f in range(SLOT):
            g = m + HALF if from_second(m, f) else m
            kept = m >= 0 and f < FEATURES and 1 <= (g - f) % FEATURES <= HALF
            rows.append(index[tuple(sorted((ORDER[f], ORDER[g])))] if kept else -1)
    return rows


def build(nc, x, ids, ids_by_field, second, tables, w1, b1, w2, b2, w3, out):
    fp32, fp32r, i32, u32 = mybir.dt.float32, mybir.dt.float32r, mybir.dt.int32, mybir.dt.uint32
    ALU, ACT = mybir.AluOpType, mybir.ActivationFunctionType

    with ExitStack() as ctx:
        def sb(name, shape, dt=fp32):
            return ctx.enter_context(nc.sbuf_tensor(name, shape, dt))

        def sem(name):
            return ctx.enter_context(nc.semaphore(name))

        ids_sb = sb("ids_sb", [P, TILES, FIELDS], i32)
        ids_row = sb("ids_row", [PICK_P, PICKS, BATCH], i32)
        row_of = sb("row_of", [PICK_P, CHUNKS], i32)
        table = sb("table", [PICK_P, PICKS, CHUNKS, DIM])
        table_hi = sb("table_hi", [PICK_P, RING, CHUNKS, DIM], fp32r)
        table_lo = sb("table_lo", [PICK_P, RING, CHUNKS, DIM], fp32r)
        onehot = sb("onehot", [PICK_P, RING, CHUNKS, BATCH], fp32r)
        picked = sb("picked", [P, TILES, GROUPS, QUAD, PICKS])
        rows = sb("rows", [P, FEATURES, DIM])
        ident = sb("ident", [P, P])
        xT = sb("xT", [P, GROUPS, QUAD, SLOT])
        second_sb = sb("second_sb", [P, HALF], i32)
        merged = sb("merged", [P, MERGED, GROUPS])
        pairs = sb("pairs", [P, STEPS, TILE])
        w1_pairs = sb("w1_pairs", [P, STEPS, H1])
        w1_dense = sb("w1_dense", [P, H1])
        w2_sb = sb("w2_sb", [P, K1, H2])
        w3_sb = sb("w3_sb", [P, K2])
        b1_sb = sb("b1_sb", [P, K1])
        b2_sb = sb("b2_sb", [P, K2])
        xdT = sb("xdT", [P, TILE])
        h1 = sb("h1", [P, K1, TILE])
        h2 = sb("h2", [P, K2, TILE])
        y_all = sb("y_all", [1, BATCH])

        tr = [ctx.enter_context(nc.psum_tensor(f"tr{i}", [P, QUAD, TILE], fp32)) for i in range(2)]
        gram = [ctx.enter_context(nc.psum_tensor(f"gram{i}", [P, CHUNK_GROUPS, P], fp32)) for i in range(2)]
        h1_ps = [ctx.enter_context(nc.psum_tensor(f"h1_ps{i}", [P, 512], fp32)) for i in range(2)]
        pick_ps = [gram[i // 2][:, 4 * (i % 2):4 * (i % 2) + 4, :] for i in range(4)]
        h2_ps = [gram[0][:, 4 * m, :] for m in range(K2)]
        y_ps = h1_ps[1][0:1, 2 * TILE:3 * TILE]

        ids_in = sem("ids_in")
        second_in = sem("second_in")
        ids_row_in = [sem(f"ids_row_in{i}") for i in range(PICKS)]
        table_in = [sem(f"table_in{i}") for i in range(PICKS)]
        w1_in = sem("w1_in")
        w_in = sem("w_in")
        dense_in = sem("dense_in")
        gathered = [sem(f"gathered{k}") for k in range(NQ)]
        ident_made = sem("ident_made")
        row_of_made = sem("row_of_made")
        pads_zeroed = sem("pads_zeroed")
        hi_made = sem("hi_made")
        lo_made = sem("lo_made")
        onehot_made = sem("onehot_made")
        pick_ready = sem("pick_ready")
        pick_taken = sem("pick_taken")
        picks_placed = sem("picks_placed")
        quad_ready = sem("quad_ready")
        quad_taken = sem("quad_taken")
        gram_ready = sem("gram_ready")
        base_made = sem("base_made")
        merge_made = sem("merge_made")
        moved_v = sem("moved_v")
        moved_s = sem("moved_s")
        h1_ready = sem("h1_ready")
        h1_made = sem("h1_made")
        h2_ready = sem("h2_ready")
        h2_made = sem("h2_made")
        y_ready = sem("y_ready")
        y_taken = sem("y_taken")
        out_done = sem("out_done")
        block = ctx.enter_context(nc.Block())

        @block.sync
        def _(sp):
            def load_dense(t):
                sp.dma_start(rows[:, DENSE_AT, :], x[bass.ts(t, TILE), :]).then_inc(dense_in, 16)

            sp.dma_start(ids_sb[:, :, :], ids).then_inc(ids_in, 16)
            for i, f in enumerate(PICKED):
                sp.dma_start(ids_row[:, i, :],
                             ids_by_field[f:f + 1, :].to_broadcast([PICK_P, BATCH])).then_inc(ids_row_in[i], 16)
                sp.dma_start(table[:, i, :, :],
                             tables[f].rearrange("(p c) d -> p c d", c=CHUNKS)).then_inc(table_in[i], 16)
                if i == 0:
                    load_dense(0)
            sp.dma_start(second_sb[:, :], second).then_inc(second_in, 16)
            sp.wait_ge(pick_ready, PICKS // 2)
            sp.dma_start(w1_pairs[:, :, :], w1[0:STEPS * P, :].rearrange("(q p) n -> p q n", p=P)).then_inc(w1_in, 16)
            sp.dma_start(w1_dense[:, :], w1[STEPS * P:, :]).then_inc(w1_in, 16)
            sp.dma_start(w2_sb[:, :, :], w2.rearrange("(q p) n -> p q n", p=P)).then_inc(w_in, 16)
            sp.dma_start(w3_sb[:, :], w3).then_inc(w_in, 16)
            sp.dma_start(b1_sb[:, :], b1).then_inc(w_in, 16)
            sp.dma_start(b2_sb[:, :], b2).then_inc(w_in, 16)
            with sp.Fori(1, TILES) as t:
                sp.wait_ge(quad_ready, t * NQ - NQ + 1)
                load_dense(t)
            sp.wait_ge(y_taken, TILES)
            sp.dma_start(out.rearrange("b o -> o b"), y_all[:, :]).then_inc(out_done, 16)
            sp.wait_ge(out_done, 16)

        @block.gpsimd
        def _(pool):
            nc.gpsimd.iota(row_of[:, :], [[1, CHUNKS]], base=0, channel_multiplier=CHUNKS).then_inc(row_of_made, 1)
            nc.gpsimd.memset(ident[:, :], 1.0).then_inc(ident_made, 1)
            pool.wait_ge(ident_made, 1)
            nc.gpsimd.affine_select(out=ident[:, :], in_=ident[:, :], compare_op=ALU.is_equal, fill=0.0,
                                    base=0, pattern=[[-1, P]], channel_multiplier=1).then_inc(ident_made, 1)

            pool.wait_ge(ids_in, 16)
            for t in range(TILES):
                for k, at in enumerate(QUADS):
                    if t >= 1:
                        pool.wait_ge(quad_ready, (t - 1) * NQ + k + 1)
                    for i in (i for i in at if i != DENSE_AT):
                        nc.gpsimd.indirect_dma_start(
                            rows[:, i, :], None, tables[ORDER[i]],
                            bass.IndirectOffsetOnAxis(ap=ids_sb[:, t, ORDER[i]:ORDER[i] + 1].bitcast(u32), axis=0),
                        ).then_inc(gathered[k], 16)

        MOVES_S, MOVES_V = (2, 3), (0, 1)

        def sources(chunk, s):
            rows_, at = slice(SLOT * s, SLOT * (s + 1)), chunk * CHUNK_GROUPS
            block_ = gram[chunk % 2][rows_, :, s * FEATURES:(s + 1) * FEATURES].rearrange("p t c -> p c t")
            return block_[:, 0:MERGED, :], block_[:, MERGED:, :], merged[rows_, :, at:at + CHUNK_GROUPS]

        def move_blocks(copy, chunk, s, blocks):
            start, end = chunk * CHUNK_GROUPS, (chunk + 1) * CHUNK_GROUPS
            for block_ in blocks:
                first = 1 if block_ < SHIFT else 0
                col = first * QUAD + block_ - SHIFT
                last = copy(pairs[SLOT * block_:SLOT * (block_ + 1), first:STEPS, s * GROUPS + start:s * GROUPS + end],
                            merged[SLOT * s:SLOT * (s + 1), col:MERGED:QUAD, start:end])
            return last

        @block.scalar
        def _(act):
            def make_hi(i):
                act.wait_ge(table_in[i], 16)
                nc.scalar.copy(table_hi[:, i % RING, :, :], table[:, i, :, :]).then_inc(hi_made, 1)

            def take_quad(t, q):
                at, bank = QUADS[q], tr[q % 2]
                act.wait_ge(quad_ready, t * NQ + q + 1)
                if DENSE_AT in at:
                    nc.scalar.copy(xdT[:, :], bank[:, 0, :])
                nc.scalar.copy(
                    xT[:, :, :, at[0]:at[0] + len(at)].rearrange("p g s f -> p s g f"),
                    bank[:, 0:len(at), :].rearrange("p f (s g) -> p s g f", s=QUAD)).then_inc(quad_taken, 1)

            def tile(t, more):
                for chunk in range(GRAM_CHUNKS):
                    act.wait_ge(gram_ready, t * GRAM_CHUNKS + chunk + 1)
                    for s in range(QUAD):
                        first_source, _, place = sources(chunk, s)
                        nc.scalar.copy(place, first_source).then_inc(base_made, 1)
                    for s in range(QUAD):
                        act.wait_ge(merge_made, (t * GRAM_CHUNKS + chunk) * QUAD + s + 1)
                        last = move_blocks(nc.scalar.copy, chunk, s, MOVES_S)
                    last.then_inc(moved_s, 1)
                if more:
                    for q in range(NQ):
                        take_quad(t + 1, q)

            for i in range(min(RING, PICKS)):
                make_hi(i)
            for i in range(PICKS):
                act.wait_ge(pick_ready, i + 1)
                if i + RING < PICKS:
                    make_hi(i + RING)
                nc.scalar.copy(picked[:, :, :, :, i].rearrange("p t g s -> p t s g"),
                               pick_ps[i % 4].rearrange("p t (s g) -> p t s g", s=QUAD)).then_inc(pick_taken, 1)
                if i < NQ:
                    take_quad(0, i)
            for q in range(PICKS, NQ):
                take_quad(0, q)
            with act.Fori(0, TILES - 1) as t:
                tile(t, True)
            tile(TILES - 1, False)

        @block.vector
        def _(dve):
            nc.vector.memset(xT[:, :, :, FEATURES:SLOT], 0.0).then_inc(pads_zeroed, 1)

            for i in range(PICKS):
                dve.wait_ge(ids_row_in[i], 16)
                if i == 0:
                    dve.wait_ge(row_of_made, 1)
                if i >= RING:
                    dve.wait_ge(pick_ready, i - RING + 1)
                for c in range(CHUNKS):
                    made = nc.vector.tensor_scalar(onehot[:, i % RING, c, :], ids_row[:, i, :], row_of[:, c:c + 1],
                                                   None, ALU.is_equal)
                    if (c + 1) % (CHUNKS // 2) == 0:
                        made.then_inc(onehot_made, 1)
                dve.wait_ge(hi_made, i + 1)
                nc.vector.tensor_tensor(table_lo[:, i % RING, :, :], table[:, i, :, :],
                                        table_hi[:, i % RING, :, :].bitcast(fp32), ALU.subtract).then_inc(lo_made, 1)
            dve.wait_ge(w_in, 16 * 4)
            dve.wait_ge(second_in, 16)

            def place_picks(t):
                nc.vector.tensor_copy(xT[:, :, :, 0:PICKS], picked[:, t, :, :, :]).then_inc(picks_placed, 1)

            dve.wait_ge(pick_taken, PICKS)
            place_picks(0)
            for t in range(TILES):
                for chunk in range(GRAM_CHUNKS):
                    for s in range(QUAD):
                        dve.wait_ge(base_made, (t * GRAM_CHUNKS + chunk) * QUAD + s + 1)
                        _, second_source, place = sources(chunk, s)
                        nc.vector.copy_predicated(
                            place[:, 1:, :],
                            second_sb[SLOT * s:SLOT * (s + 1), :].unsqueeze(2).to_broadcast(
                                [SLOT, HALF, CHUNK_GROUPS]),
                            second_source).then_inc(merge_made, 1)
                    for s in range(QUAD):
                        dve.wait_ge(merge_made, (t * GRAM_CHUNKS + chunk) * QUAD + s + 1)
                        last = move_blocks(nc.vector.tensor_copy, chunk, s, MOVES_V)
                    last.then_inc(moved_v, 1)
                if t + 1 < TILES:
                    place_picks(t + 1)
                for half in range(2):
                    dve.wait_ge(h1_ready, 2 * t + half + 1)
                    for n in (0, 1):
                        k = 2 * half + n
                        nc.vector.tensor_scalar(h1[:, k, :], h1_ps[half][:, n * TILE:(n + 1) * TILE],
                                                b1_sb[:, k:k + 1], 0.0, ALU.add, ALU.max).then_inc(h1_made, 1)
                for m in range(K2):
                    dve.wait_ge(h2_ready, K2 * t + m + 1)
                    nc.vector.tensor_scalar(h2[:, m, :], h2_ps[m], b2_sb[:, m:m + 1], 0.0,
                                            ALU.add, ALU.max).then_inc(h2_made, 1)
                dve.wait_ge(y_ready, t + 1)
                nc.vector.tensor_copy(y_all[:, bass.ts(t, TILE)], y_ps).then_inc(y_taken, 1)

        @block.tensor
        def _(pe):
            def pick(i):
                if i >= 4:
                    pe.wait_ge(pick_taken, i - 3)
                pe.wait_ge(hi_made, i + 1)
                for part, tab in enumerate((table_hi, table_lo)):
                    if part == 1:
                        pe.wait_ge(lo_made, i + 1)
                    for c in range(CHUNKS):
                        if part == 0 and c % (CHUNKS // 2) == 0:
                            pe.wait_ge(onehot_made, 2 * i + 1 + c // (CHUNKS // 2))
                        last = nc.tensor.matmul(pick_ps[i % 4], tab[:, i % RING, c, :], onehot[:, i % RING, c, :],
                                                start=(c == 0 and part == 0), stop=(c == CHUNKS - 1 and part == 1))
                last.then_inc(pick_ready, 1)

            def quad(t, q):
                at, bank = QUADS[q], tr[q % 2]
                if q == 0:
                    pe.wait_ge(dense_in, t * 16 + 16)
                n_rows = len(at) - (q == 0)
                pe.wait_ge(gathered[q], t * (16 * n_rows) + 16 * n_rows)
                if q >= 2:
                    pe.wait_ge(quad_taken, t * NQ + q - 1)
                for n, i in enumerate(at):
                    last = nc.tensor.transpose(bank[:, n, :], rows[:, i, :], ident[:, :])
                last.then_inc(quad_ready, 1)

            def tile(t, more):
                pe.wait_ge(picks_placed, t + 1)
                pe.wait_ge(quad_taken, t * NQ + NQ)
                for chunk in range(GRAM_CHUNKS):
                    if chunk >= 2:
                        pe.wait_ge(merge_made, (t * GRAM_CHUNKS + chunk - 1) * QUAD)
                    for n in range(CHUNK_GROUPS):
                        g = chunk * CHUNK_GROUPS + n
                        last = nc.tensor.matmul(gram[chunk % 2][:, n, 0:QUAD * FEATURES], xT[:, g, :, :],
                                                xT[:, g, :, 0:FEATURES], start=True, stop=True)
                    last.then_inc(gram_ready, 1)

                pe.wait_ge(w1_in, 16 * 2)
                h1_out = [h1_ps[k // 2][:, (k % 2) * TILE:(k % 2 + 1) * TILE] for k in range(K1)]
                for k in range(K1):
                    nc.tensor.matmul(h1_out[k], w1_dense[:, k * P:(k + 1) * P], xdT[:, :],
                                     start=(k % 2 == 0), stop=False, skip_group_check=True)
                if more:
                    for q in (0, 1, 2):
                        quad(t + 1, q)
                pe.wait_ge(moved_v, t * GRAM_CHUNKS + GRAM_CHUNKS)
                pe.wait_ge(moved_s, t * GRAM_CHUNKS + GRAM_CHUNKS)
                for k in range(K1):
                    for q in range(STEPS):
                        low = SLOT * SHIFT if q == 0 else 0
                        last = nc.tensor.matmul(h1_out[k], w1_pairs[low:P, q, k * P:(k + 1) * P], pairs[low:P, q, :],
                                                start=False, stop=(q == STEPS - 1), skip_group_check=True)
                    if k % 2:
                        last.then_inc(h1_ready, 1)
                if more:
                    quad(t + 1, 3)

                pe.wait_ge(w_in, 16 * 4)
                for k in range(K1):
                    if more and k == K1 // 2:
                        quad(t + 1, 4)
                    pe.wait_ge(h1_made, t * K1 + k + 1)
                    for m in range(K2):
                        last = nc.tensor.matmul(h2_ps[m], w2_sb[:, k, m * P:(m + 1) * P], h1[:, k, :],
                                                start=(k == 0), stop=(k == K1 - 1))
                        if k == K1 - 1:
                            last.then_inc(h2_ready, 1)
                if more:
                    quad(t + 1, 5)

                for m in range(K2):
                    pe.wait_ge(h2_made, t * K2 + m + 1)
                    last = nc.tensor.matmul(y_ps, w3_sb[:, m:m + 1], h2[:, m, :], start=(m == 0), stop=(m == K2 - 1))
                last.then_inc(y_ready, 1)

            pe.wait_ge(ident_made, 2)
            pe.wait_ge(pads_zeroed, 1)
            for i in range(PICKS):
                pick(i)
                if i < NQ:
                    quad(0, i)
            for q in range(PICKS, NQ):
                quad(0, q)
            with pe.Fori(0, TILES - 1) as t:
                tile(t, True)
            tile(TILES - 1, False)


def kernel(**inputs):
    import numpy as np
    import concourse.bacc as bacc
    from concourse.bass_utils import run_bass_kernel_spmd

    nc = bacc.Bacc("TRN2", target_bir_lowering=False, num_devices=1)
    arrays = {}

    def dram(name, a):
        a = np.ascontiguousarray(a)
        arrays[f"in_{name}_dram"] = a
        return nc.dram_tensor(f"in_{name}_dram", a.shape, mybir.dt.from_np(a.dtype), kind="ExternalInput").ap()

    ids = np.asarray(inputs["ids"])
    w1 = np.asarray(inputs["W_top1"])
    chosen = np.array(pair_rows())
    n_pairs = FEATURES * (FEATURES - 1) // 2
    w1_padded = np.zeros((STEPS * P + DIM, H1), w1.dtype)
    w1_padded[np.flatnonzero(chosen >= 0)] = w1[chosen[chosen >= 0]]
    w1_padded[STEPS * P:] = w1[n_pairs:]

    second = np.array([[from_second(m, f) for m in range(1, MERGED)] for f in range(SLOT)] * QUAD, np.int32)

    def by_partition(v):
        return np.asarray(v).reshape(-1, P).T

    out = nc.dram_tensor("out_dram", (BATCH, 1), mybir.dt.float32, kind="ExternalOutput").ap()
    build(nc, dram("x", inputs["r_dense_x"]), dram("ids", ids.reshape(TILES, P, FIELDS).transpose(1, 0, 2)), dram("ids_by_field", ids.T),
          dram("second", second),
          [dram(f"tbl_{f}", inputs[f"tbl_{f}"]) for f in range(FIELDS)],
          dram("w1", w1_padded), dram("b1", by_partition(inputs["b_top1"])), dram("w2", inputs["W_top2"]),
          dram("b2", by_partition(inputs["b_top2"])), dram("w3", by_partition(inputs["W_top3"])), out)
    r = run_bass_kernel_spmd(nc, [arrays], core_ids=[0])
    return r.results[0]["out_dram"]
```

```python
from contextlib import ExitStack

import concourse.bass as bass
from concourse import mybir

BATCH, DIM, FIELDS = 512, 128, 26
ROWS = [12500, 125000, 1000, 1250, 12500, 1250, 1250, 12500, 1250, 12500, 12500, 12500, 1000,
        12500, 1000, 1250, 1000, 1250, 1250, 1000, 1250, 12500, 1000, 1000, 1000, 1000]
H1, H2 = 512, 256

P = 128
TILE = 128
TILES = BATCH // TILE
FEATURES = FIELDS + 1
SLOT = 32
QUAD = 4

PICK_ROWS = 1000
PICKED = [f for f in range(FIELDS) if ROWS[f] == PICK_ROWS][:7]
CHUNKS = 8
PICK_P = PICK_ROWS // CHUNKS
GATHERED = [f for f in range(FIELDS) if f not in PICKED]
ORDER = PICKED + [FIELDS] + GATHERED
PICKS = len(PICKED)
DVE_CHUNKS = CHUNKS - 1
ACT_CHUNKS = CHUNKS - DVE_CHUNKS
RING = 3
WARMUPS = 10
DENSE_AT = PICKS

QUADS = [list(range(a, min(a + QUAD, FEATURES - 1))) for a in range(DENSE_AT, FEATURES - 1, QUAD)]
QUADS += [[FEATURES - 1]]
NQ = len(QUADS)
FIRST_QUADS = [[i - 1] if 1 <= i < PICKS - 1 else [] for i in range(PICKS)]
FIRST_QUADS[-1] = list(range(PICKS - 2, NQ))

GROUPS = TILE // QUAD
CHUNK_GROUPS = 8
GRAM_CHUNKS = GROUPS // CHUNK_GROUPS
HALF = (FEATURES - 1) // 2
MERGED = HALF + 1
SHIFT = (-MERGED) % QUAD
STEPS = (MERGED + SHIFT) // QUAD
K1 = H1 // P
K2 = H2 // P


def from_second(m, f):
    return m >= 1 and m <= f < m + HALF


def pair_rows():
    index = {}
    for i in range(FEATURES):
        for j in range(i + 1, FEATURES):
            index[i, j] = len(index)
    rows = []
    for at in range(STEPS * QUAD):
        m = at - SHIFT
        for f in range(SLOT):
            g = m + HALF if from_second(m, f) else m
            kept = m >= 0 and f < FEATURES and 1 <= (g - f) % FEATURES <= HALF
            rows.append(index[tuple(sorted((ORDER[f], ORDER[g])))] if kept else -1)
    return rows


def build(nc, x, ids, ids_by_field, second, tables, w1, b1, w2, b2, w3, out):
    fp32, fp32r, i32, u32 = mybir.dt.float32, mybir.dt.float32r, mybir.dt.int32, mybir.dt.uint32
    ALU, ACT = mybir.AluOpType, mybir.ActivationFunctionType

    with ExitStack() as ctx:
        def sb(name, shape, dt=fp32):
            return ctx.enter_context(nc.sbuf_tensor(name, shape, dt))

        def sem(name):
            return ctx.enter_context(nc.semaphore(name))

        ids_sb = sb("ids_sb", [P, TILES, FIELDS], i32)
        ids_row = sb("ids_row", [PICK_P, PICKS, BATCH], i32)
        row_of = sb("row_of", [PICK_P, CHUNKS], i32)
        row_f = sb("row_f", [PICK_P, CHUNKS])
        off2 = sb("off2", [PICK_P, 2, BATCH])
        table = sb("table", [PICK_P, PICKS, CHUNKS, DIM])
        table_hi = sb("table_hi", [PICK_P, RING, CHUNKS, DIM], fp32r)
        table_lo = sb("table_lo", [PICK_P, RING, CHUNKS, DIM], fp32r)
        onehot = sb("onehot", [PICK_P, RING, CHUNKS, BATCH], fp32r)
        picked = sb("picked", [P, TILES, GROUPS, QUAD, PICKS])
        rows = sb("rows", [P, FEATURES, DIM])
        ident = sb("ident", [P, P])
        xT = sb("xT", [P, GROUPS, QUAD, SLOT])
        second_sb = sb("second_sb", [P, HALF], i32)
        merged = sb("merged", [P, MERGED, GROUPS])
        pairs = sb("pairs", [P, STEPS, TILE])
        w1_pairs = sb("w1_pairs", [P, STEPS, H1])
        w1_dense = sb("w1_dense", [P, H1])
        w2_sb = sb("w2_sb", [P, K1, H2])
        w3_sb = sb("w3_sb", [P, K2])
        b1_sb = sb("b1_sb", [P, K1])
        b2_sb = sb("b2_sb", [P, K2])
        xdT = sb("xdT", [P, TILE])
        h1 = sb("h1", [P, K1, TILE])
        h2 = sb("h2", [P, K2, TILE])
        y_all = sb("y_all", [1, BATCH])

        tr = [ctx.enter_context(nc.psum_tensor(f"tr{i}", [P, QUAD, TILE], fp32)) for i in range(2)]
        gram = [ctx.enter_context(nc.psum_tensor(f"gram{i}", [P, CHUNK_GROUPS, P], fp32)) for i in range(2)]
        h1_ps = [ctx.enter_context(nc.psum_tensor(f"h1_ps{i}", [P, 512], fp32)) for i in range(2)]
        pick_ps = [gram[i // 2][:, 4 * (i % 2):4 * (i % 2) + 4, :] for i in range(4)]
        h2_ps = [gram[0][:, 4 * m, :] for m in range(K2)]
        y_ps = h1_ps[1][0:1, 2 * TILE:3 * TILE]

        ids_in = sem("ids_in")
        second_in = sem("second_in")
        ids_row_in = [sem(f"ids_row_in{i}") for i in range(PICKS)]
        table_in = [sem(f"table_in{i}") for i in range(PICKS)]
        w1_in = sem("w1_in")
        w_in = sem("w_in")
        dense_in = sem("dense_in")
        gathered = [sem(f"gathered{k}") for k in range(NQ)]
        ident_made = sem("ident_made")
        row_of_made = sem("row_of_made")
        pads_zeroed = sem("pads_zeroed")
        hi_made = sem("hi_made")
        lo_made = sem("lo_made")
        row_f_made = sem("row_f_made")
        onehot_made = sem("onehot_made")
        off2_made = sem("off2_made")
        onehot_made_s = sem("onehot_made_s")
        pick_ready = sem("pick_ready")
        pick_taken = sem("pick_taken")
        picks_placed = sem("picks_placed")
        last_pick_placed = sem("last_pick_placed")
        quad_ready = sem("quad_ready")
        quad_taken = sem("quad_taken")
        gram_ready = sem("gram_ready")
        base_made = sem("base_made")
        merge_made = sem("merge_made")
        moved_v = sem("moved_v")
        moved_s = sem("moved_s")
        h1_ready = sem("h1_ready")
        h1_made = sem("h1_made")
        h2_ready = sem("h2_ready")
        h2_made = sem("h2_made")
        y_ready = sem("y_ready")
        y_taken = sem("y_taken")
        out_done = sem("out_done")
        block = ctx.enter_context(nc.Block())

        @block.sync
        def _(sp):
            def load_dense(t):
                sp.dma_start(rows[:, DENSE_AT, :], x[bass.ts(t, TILE), :]).then_inc(dense_in, 16)

            sp.dma_start(ids_sb[:, :, :], ids).then_inc(ids_in, 16)
            for i, f in enumerate(PICKED):
                if i > RING:
                    sp.wait_ge(pick_ready, i - RING)
                sp.dma_start(ids_row[:, i, :],
                             ids_by_field[f:f + 1, :].to_broadcast([PICK_P, BATCH])).then_inc(ids_row_in[i], 16)
                sp.dma_start(table[:, i, :, :],
                             tables[f].rearrange("(p c) d -> p c d", c=CHUNKS)).then_inc(table_in[i], 16)
                if i == 0:
                    load_dense(0)
            sp.dma_start(second_sb[:, :], second).then_inc(second_in, 16)
            sp.wait_ge(pick_ready, PICKS - 2)
            sp.dma_start(w1_pairs[:, :, :], w1[0:STEPS * P, :].rearrange("(q p) n -> p q n", p=P)).then_inc(w1_in, 16)
            sp.dma_start(w1_dense[:, :], w1[STEPS * P:, :]).then_inc(w1_in, 16)
            sp.dma_start(w2_sb[:, :, :], w2.rearrange("(q p) n -> p q n", p=P)).then_inc(w_in, 16)
            sp.dma_start(w3_sb[:, :], w3).then_inc(w_in, 16)
            sp.dma_start(b1_sb[:, :], b1).then_inc(w_in, 16)
            sp.dma_start(b2_sb[:, :], b2).then_inc(w_in, 16)
            with sp.Fori(1, TILES) as t:
                sp.wait_ge(quad_ready, t * NQ - NQ + 1)
                load_dense(t)
            sp.wait_ge(y_taken, TILES)
            sp.dma_start(out.rearrange("b o -> o b"), y_all[:, :]).then_inc(out_done, 16)
            sp.wait_ge(out_done, 16)

        @block.gpsimd
        def _(pool):
            nc.gpsimd.iota(row_of[:, :], [[1, CHUNKS]], base=0, channel_multiplier=CHUNKS).then_inc(row_of_made, 1)
            nc.gpsimd.memset(ident[:, :], 1.0).then_inc(ident_made, 1)
            pool.wait_ge(ident_made, 1)
            nc.gpsimd.affine_select(out=ident[:, :], in_=ident[:, :], compare_op=ALU.is_equal, fill=0.0,
                                    base=0, pattern=[[-1, P]], channel_multiplier=1).then_inc(ident_made, 1)

            pool.wait_ge(ids_in, 16)
            for t in range(TILES):
                for k, at in enumerate(QUADS):
                    if t >= 1:
                        pool.wait_ge(quad_ready, (t - 1) * NQ + k + 1)
                    for i in (i for i in at if i != DENSE_AT):
                        nc.gpsimd.indirect_dma_start(
                            rows[:, i, :], None, tables[ORDER[i]],
                            bass.IndirectOffsetOnAxis(ap=ids_sb[:, t, ORDER[i]:ORDER[i] + 1].bitcast(u32), axis=0),
                        ).then_inc(gathered[k], 16)

        MOVES_S, MOVES_V = (2, 3), (0, 1)

        def sources(chunk, s):
            rows_, at = slice(SLOT * s, SLOT * (s + 1)), chunk * CHUNK_GROUPS
            block_ = gram[chunk % 2][rows_, :, s * FEATURES:(s + 1) * FEATURES].rearrange("p t c -> p c t")
            return block_[:, 0:MERGED, :], block_[:, MERGED:, :], merged[rows_, :, at:at + CHUNK_GROUPS]

        def move_blocks(copy, chunk, s, blocks):
            start, end = chunk * CHUNK_GROUPS, (chunk + 1) * CHUNK_GROUPS
            for block_ in blocks:
                first = 1 if block_ < SHIFT else 0
                col = first * QUAD + block_ - SHIFT
                last = copy(pairs[SLOT * block_:SLOT * (block_ + 1), first:STEPS, s * GROUPS + start:s * GROUPS + end],
                            merged[SLOT * s:SLOT * (s + 1), col:MERGED:QUAD, start:end])
            return last

        @block.scalar
        def _(act):
            def make_hi(i):
                act.wait_ge(table_in[i], 16)
                for half in (slice(0, CHUNKS // 2), slice(CHUNKS // 2, CHUNKS)):
                    nc.scalar.copy(table_hi[:, i % RING, half, :], table[:, i, half, :]).then_inc(hi_made, 1)

            def make_onehot(i):
                act.wait_ge(ids_row_in[i], 16)
                for c in range(DVE_CHUNKS, CHUNKS):
                    done = i * ACT_CHUNKS + c - DVE_CHUNKS
                    if done >= 2:
                        act.wait_ge(onehot_made_s, done - 1)
                    nc.scalar.activation(off2[:, done % 2, :], ids_row[:, i, :], ACT.Square, bias=row_f[:, c:c + 1],
                                         scale=-1.0).then_inc(off2_made, 1)
                    act.wait_ge(off2_made, done + 1)
                    nc.scalar.activation(onehot[:, i % RING, c, :], off2[:, done % 2, :], ACT.Relu, bias=1.0,
                                         scale=-1.0).then_inc(onehot_made_s, 1)

            def take_quad(t, q):
                at, bank = QUADS[q], tr[q % 2]
                act.wait_ge(quad_ready, t * NQ + q + 1)
                if DENSE_AT in at:
                    nc.scalar.copy(xdT[:, :], bank[:, 0, :])
                nc.scalar.copy(
                    xT[:, :, :, at[0]:at[0] + len(at)].rearrange("p g s f -> p s g f"),
                    bank[:, 0:len(at), :].rearrange("p f (s g) -> p s g f", s=QUAD)).then_inc(quad_taken, 1)

            def tile(t, more):
                for chunk in range(GRAM_CHUNKS):
                    act.wait_ge(gram_ready, t * GRAM_CHUNKS + chunk + 1)
                    for s in range(QUAD):
                        first_source, _, place = sources(chunk, s)
                        nc.scalar.copy(place, first_source).then_inc(base_made, 1)
                    for s in range(QUAD):
                        act.wait_ge(merge_made, (t * GRAM_CHUNKS + chunk) * QUAD + s + 1)
                        last = move_blocks(nc.scalar.copy, chunk, s, MOVES_S)
                    last.then_inc(moved_s, 1)
                if more:
                    for q in range(NQ):
                        take_quad(t + 1, q)

            for i in range(RING):
                make_hi(i)
                if i == 0:
                    act.wait_ge(row_f_made, 1)
                make_onehot(i)
            for i in range(PICKS):
                act.wait_ge(pick_ready, i + 1)
                if i + RING < PICKS:
                    make_hi(i + RING)
                    make_onehot(i + RING)
                columns = pick_ps[i % 4].rearrange("p t (s g) -> p t s g", s=QUAD)
                start = 0
                if i == PICKS - 1:
                    nc.scalar.copy(xT[:, :, :, i].rearrange("p g s -> p s g"), columns[:, 0, :, :]).then_inc(
                        last_pick_placed, 1)
                    start = 1
                nc.scalar.copy(picked[:, start:, :, :, i].rearrange("p t g s -> p t s g"),
                               columns[:, start:, :, :]).then_inc(pick_taken, 1)
                for q in FIRST_QUADS[i]:
                    take_quad(0, q)
            with act.Fori(0, TILES - 1) as t:
                tile(t, True)
            tile(TILES - 1, False)

        @block.vector
        def _(dve):
            nc.vector.memset(xT[:, :, :, FEATURES:SLOT], 0.0).then_inc(pads_zeroed, 1)

            dve.wait_ge(row_of_made, 1)
            nc.vector.tensor_copy(row_f[:, :], row_of[:, :]).then_inc(row_f_made, 1)
            for i in range(PICKS):
                dve.wait_ge(ids_row_in[i], 16)
                if i >= RING:
                    dve.wait_ge(pick_ready, i - RING + 1)
                for c in range(DVE_CHUNKS):
                    made = nc.vector.tensor_scalar(onehot[:, i % RING, c, :], ids_row[:, i, :], row_of[:, c:c + 1],
                                                   None, ALU.is_equal)
                    if c + 1 in (CHUNKS // 2, DVE_CHUNKS):
                        made.then_inc(onehot_made, 1)
                dve.wait_ge(hi_made, 2 * i + 2)
                nc.vector.tensor_tensor(table_lo[:, i % RING, :, :], table[:, i, :, :],
                                        table_hi[:, i % RING, :, :].bitcast(fp32), ALU.subtract).then_inc(lo_made, 1)
            dve.wait_ge(w_in, 16 * 4)
            dve.wait_ge(second_in, 16)

            def place_picks(t, picks):
                nc.vector.tensor_copy(xT[:, :, :, 0:picks], picked[:, t, :, :, 0:picks]).then_inc(picks_placed, 1)

            dve.wait_ge(pick_taken, PICKS - 1)
            place_picks(0, PICKS - 1)
            dve.wait_ge(pick_taken, PICKS)
            for t in range(TILES):
                for chunk in range(GRAM_CHUNKS):
                    for s in range(QUAD):
                        dve.wait_ge(base_made, (t * GRAM_CHUNKS + chunk) * QUAD + s + 1)
                        _, second_source, place = sources(chunk, s)
                        nc.vector.copy_predicated(
                            place[:, 1:, :],
                            second_sb[SLOT * s:SLOT * (s + 1), :].unsqueeze(2).to_broadcast(
                                [SLOT, HALF, CHUNK_GROUPS]),
                            second_source).then_inc(merge_made, 1)
                    for s in range(QUAD):
                        dve.wait_ge(merge_made, (t * GRAM_CHUNKS + chunk) * QUAD + s + 1)
                        last = move_blocks(nc.vector.tensor_copy, chunk, s, MOVES_V)
                    last.then_inc(moved_v, 1)
                if t + 1 < TILES:
                    place_picks(t + 1, PICKS)
                for half in range(2):
                    dve.wait_ge(h1_ready, 2 * t + half + 1)
                    for n in (0, 1):
                        k = 2 * half + n
                        nc.vector.tensor_scalar(h1[:, k, :], h1_ps[half][:, n * TILE:(n + 1) * TILE],
                                                b1_sb[:, k:k + 1], 0.0, ALU.add, ALU.max).then_inc(h1_made, 1)
                for m in range(K2):
                    dve.wait_ge(h2_ready, K2 * t + m + 1)
                    nc.vector.tensor_scalar(h2[:, m, :], h2_ps[m], b2_sb[:, m:m + 1], 0.0,
                                            ALU.add, ALU.max).then_inc(h2_made, 1)
                dve.wait_ge(y_ready, t + 1)
                nc.vector.tensor_copy(y_all[:, bass.ts(t, TILE)], y_ps).then_inc(y_taken, 1)

        @block.tensor
        def _(pe):
            def pick(i):
                if i >= 4:
                    pe.wait_ge(pick_taken, i - 3)
                for part, tab in enumerate((table_hi, table_lo)):
                    if part == 1:
                        pe.wait_ge(lo_made, i + 1)
                    for c in range(CHUNKS):
                        if part == 0 and c % (CHUNKS // 2) == 0:
                            pe.wait_ge(hi_made, 2 * i + 1 + c // (CHUNKS // 2))
                            pe.wait_ge(onehot_made, 2 * i + 1 + c // (CHUNKS // 2))
                        if part == 0 and c >= DVE_CHUNKS:
                            pe.wait_ge(onehot_made_s, i * ACT_CHUNKS + c - DVE_CHUNKS + 1)
                        last = nc.tensor.matmul(pick_ps[i % 4], tab[:, i % RING, c, :], onehot[:, i % RING, c, :],
                                                start=(c == 0 and part == 0), stop=(c == CHUNKS - 1 and part == 1))
                last.then_inc(pick_ready, 1)

            def quad(t, q):
                at, bank = QUADS[q], tr[q % 2]
                if q == 0:
                    pe.wait_ge(dense_in, t * 16 + 16)
                n_rows = len(at) - (q == 0)
                pe.wait_ge(gathered[q], t * (16 * n_rows) + 16 * n_rows)
                if q >= 2:
                    pe.wait_ge(quad_taken, t * NQ + q - 1)
                for n, i in enumerate(at):
                    last = nc.tensor.transpose(bank[:, n, :], rows[:, i, :], ident[:, :])
                last.then_inc(quad_ready, 1)

            def tile(t, more):
                pe.wait_ge(picks_placed, t + 1)
                pe.wait_ge(quad_taken, t * NQ + NQ)
                for chunk in range(GRAM_CHUNKS):
                    if chunk == 1:
                        pe.wait_ge(pick_taken, PICKS)
                    if chunk >= 2:
                        pe.wait_ge(merge_made, (t * GRAM_CHUNKS + chunk - 1) * QUAD)
                    for n in range(CHUNK_GROUPS):
                        g = chunk * CHUNK_GROUPS + n
                        last = nc.tensor.matmul(gram[chunk % 2][:, n, 0:QUAD * FEATURES], xT[:, g, :, :],
                                                xT[:, g, :, 0:FEATURES], start=True, stop=True)
                    last.then_inc(gram_ready, 1)

                pe.wait_ge(w1_in, 16 * 2)
                h1_out = [h1_ps[k // 2][:, (k % 2) * TILE:(k % 2 + 1) * TILE] for k in range(K1)]
                for k in range(K1):
                    nc.tensor.matmul(h1_out[k], w1_dense[:, k * P:(k + 1) * P], xdT[:, :],
                                     start=(k % 2 == 0), stop=False, skip_group_check=True)
                if more:
                    for q in (0, 1):
                        quad(t + 1, q)
                pe.wait_ge(moved_v, t * GRAM_CHUNKS + GRAM_CHUNKS)
                pe.wait_ge(moved_s, t * GRAM_CHUNKS + GRAM_CHUNKS)
                for k in range(K1):
                    if more and k == K1 // 2:
                        quad(t + 1, 2)
                    for q in range(STEPS):
                        low = SLOT * SHIFT if q == 0 else 0
                        last = nc.tensor.matmul(h1_out[k], w1_pairs[low:P, q, k * P:(k + 1) * P], pairs[low:P, q, :],
                                                start=False, stop=(q == STEPS - 1), skip_group_check=True)
                    if k % 2:
                        last.then_inc(h1_ready, 1)
                if more:
                    quad(t + 1, 3)

                pe.wait_ge(w_in, 16 * 4)
                for k in range(K1):
                    pe.wait_ge(h1_made, t * K1 + k + 1)
                    for m in range(K2):
                        last = nc.tensor.matmul(h2_ps[m], w2_sb[:, k, m * P:(m + 1) * P], h1[:, k, :],
                                                start=(k == 0), stop=(k == K1 - 1))
                        if k == K1 - 1:
                            last.then_inc(h2_ready, 1)
                if more:
                    quad(t + 1, 4)

                for m in range(K2):
                    pe.wait_ge(h2_made, t * K2 + m + 1)
                    last = nc.tensor.matmul(y_ps, w3_sb[:, m:m + 1], h2[:, m, :], start=(m == 0), stop=(m == K2 - 1))
                last.then_inc(y_ready, 1)
                if more:
                    quad(t + 1, 5)

            pe.wait_ge(ident_made, 2)
            for _ in range(WARMUPS):
                nc.tensor.matmul(tr[1][:, 0, :], ident[:, :], ident[:, :], start=True, stop=True)
            pe.wait_ge(pads_zeroed, 1)
            for i in range(PICKS):
                pick(i)
                for q in FIRST_QUADS[i]:
                    quad(0, q)
            pe.wait_ge(last_pick_placed, 1)
            with pe.Fori(0, TILES - 1) as t:
                tile(t, True)
            tile(TILES - 1, False)


def kernel(**inputs):
    import numpy as np
    import concourse.bacc as bacc
    from concourse.bass_utils import run_bass_kernel_spmd

    nc = bacc.Bacc("TRN2", target_bir_lowering=False, num_devices=1)
    arrays = {}

    def dram(name, a):
        a = np.ascontiguousarray(a)
        arrays[f"in_{name}_dram"] = a
        return nc.dram_tensor(f"in_{name}_dram", a.shape, mybir.dt.from_np(a.dtype), kind="ExternalInput").ap()

    ids = np.asarray(inputs["ids"])
    w1 = np.asarray(inputs["W_top1"])
    chosen = np.array(pair_rows())
    n_pairs = FEATURES * (FEATURES - 1) // 2
    w1_padded = np.zeros((STEPS * P + DIM, H1), w1.dtype)
    w1_padded[np.flatnonzero(chosen >= 0)] = w1[chosen[chosen >= 0]]
    w1_padded[STEPS * P:] = w1[n_pairs:]

    second = np.array([[from_second(m, f) for m in range(1, MERGED)] for f in range(SLOT)] * QUAD, np.int32)

    def by_partition(v):
        return np.asarray(v).reshape(-1, P).T

    out = nc.dram_tensor("out_dram", (BATCH, 1), mybir.dt.float32, kind="ExternalOutput").ap()
    build(nc, dram("x", inputs["r_dense_x"]), dram("ids", ids.reshape(TILES, P, FIELDS).transpose(1, 0, 2)),
          dram("ids_by_field", ids.T), dram("second", second),
          [dram(f"tbl_{f}", inputs[f"tbl_{f}"]) for f in range(FIELDS)],
          dram("w1", w1_padded), dram("b1", by_partition(inputs["b_top1"])), dram("w2", inputs["W_top2"]),
          dram("b2", by_partition(inputs["b_top2"])), dram("w3", by_partition(inputs["W_top3"])), out)
    r = run_bass_kernel_spmd(nc, [arrays], core_ids=[0])
    return r.results[0]["out_dram"]
```
